# Optimizing a Trainium2 kernel written in Bass

```python
import numpy as np
import jax
import jax.numpy as jnp

def _softmax(x, axis=-1):
    return jax.nn.softmax(x, axis=axis)

def _gelu(x):
    return jax.nn.gelu(x, approximate=True)

def _silu(x):
    return jax.nn.silu(x)

def _sigmoid(x):
    return jax.nn.sigmoid(x)

def _layernorm(x, axis=-1, eps=1e-05):
    m = jnp.mean(x, axis=axis, keepdims=True)
    v = jnp.var(x, axis=axis, keepdims=True)
    return (x - m) / jnp.sqrt(v + eps)

def _scatter_add(tgt, idx, src, axis=0):
    return tgt.at[idx].add(src)

def _segment_sum(src, seg, n):
    return jax.ops.segment_sum(src, seg, n)
kernel_name = 'mk_cond_seq_d1_seqx_r4_557c2a'

def setup_inputs(seed: int=0):
    np.random.seed(seed)
    _w = jnp.asarray

    def _rec_inputs():
        import jax
        import jax.numpy as jnp
        _rk = jax.random.key(seed)
        x = -1.528e-05 + 0.9999 * jax.random.normal(jax.random.fold_in(_rk, 1), (64, 64, 512), jnp.float32)
        _lenS = 64 - jax.random.randint(jax.random.fold_in(_rk, 7), (64,), 0, max(1, 64 // 4) + 1, jnp.int32)
        _lenS2 = 64 - jax.random.randint(jax.random.fold_in(_rk, 8), (64,), 0, max(1, 64 // 4) + 1, jnp.int32)
        itok_B_1_2 = jax.random.randint(jax.random.fold_in(_rk, 11), (64,), 1, 3, jnp.int32)
        return (x, itok_B_1_2)
    x, itok_B_1_2 = _rec_inputs()

    def _L0_cond_setup():
        import jax, jax.numpy as jnp
        import numpy as np
        B, S, H = (8, 512, 512)
        BN = 256
        E = 3
        LN_EPS = 1e-05
        key = jax.random.key(seed)
        ks = jax.random.split(key, 8)
        stream = jax.random.randint(ks[0], (B,), 0, E, dtype=jnp.int32)
        hidden_states = jax.random.normal(ks[1], (B, S, H), dtype=jnp.float32)
        W_down = jax.random.normal(ks[2], (E, H, BN), dtype=jnp.float32) * 0.02
        b_down = jnp.zeros((E, BN), dtype=jnp.float32)
        W_up = jax.random.normal(ks[3], (E, BN, H), dtype=jnp.float32) * 0.02
        b_up = jnp.zeros((E, H), dtype=jnp.float32)
        ln_w = jnp.ones((E, H), dtype=jnp.float32)
        ln_b = jnp.zeros((E, H), dtype=jnp.float32)
        return {'stream': stream, 'hidden_states': hidden_states, 'W_down': W_down, 'b_down': b_down, 'W_up': W_up, 'b_up': b_up, 'ln_w': ln_w, 'ln_b': ln_b}
    _L0_cond_all = _L0_cond_setup()
    _L0_cond_in = {k: v for k, v in _L0_cond_all.items() if k in ('W_down', 'b_down', 'W_up', 'b_up', 'ln_w', 'ln_b')}
    del _L0_cond_all
    return {'x': x, 'itok_B_1_2': itok_B_1_2, 'L0_cond_W_down': _L0_cond_in['W_down'], 'L0_cond_b_down': _L0_cond_in['b_down'], 'L0_cond_W_up': _L0_cond_in['W_up'], 'L0_cond_b_up': _L0_cond_in['b_up'], 'L0_cond_ln_w': _L0_cond_in['ln_w'], 'L0_cond_ln_b': _L0_cond_in['ln_b']}

def reference(x, itok_B_1_2, L0_cond_W_down, L0_cond_b_down, L0_cond_W_up, L0_cond_b_up, L0_cond_ln_w, L0_cond_ln_b):
    import jax
    import jax.numpy as jnp

    def _L0_cond_ref(stream, hidden_states, W_down, b_down, W_up, b_up, ln_w, ln_b):
        import jax, jax.numpy as jnp
        import numpy as np
        B, S, H = (8, 512, 512)
        BN = 256
        E = 3
        LN_EPS = 1e-05
        Wd = W_down[stream]
        bd = b_down[stream]
        Wu = W_up[stream]
        bu = b_up[stream]
        g = ln_w[stream]
        b = ln_b[stream]
        residual = hidden_states
        h = jnp.einsum('bsh,bhk->bsk', hidden_states, Wd) + bd[:, None, :]
        h = jax.nn.gelu(h, approximate=False)
        h = jnp.einsum('bsk,bkh->bsh', h, Wu) + bu[:, None, :]
        h = residual + h
        mean = jnp.mean(h, axis=-1, keepdims=True)
        var = jnp.mean(jnp.square(h - mean), axis=-1, keepdims=True)
        h = (h - mean) * jax.lax.rsqrt(var + LN_EPS)
        return h * g[:, None, :] + b[:, None, :]
    x = _L0_cond_ref(itok_B_1_2, x, L0_cond_W_down, L0_cond_b_down, L0_cond_W_up, L0_cond_b_up, L0_cond_ln_w, L0_cond_ln_b)
    return x

_drawn_inputs = setup_inputs


def setup_inputs(seed=0):
    import zlib

    import numpy as np

    out = dict(_drawn_inputs(seed))
    spreads = {'L0_cond_b_down': (0.0, 0.413),
     'L0_cond_b_up': (0.0, 0.1),
     'L0_cond_ln_w': (1.0, 0.2),
     'L0_cond_ln_b': (0.0, 0.1)}
    factors = {}
    for name, (base, spread) in spreads.items():
        noise = np.random.default_rng([zlib.crc32(name.encode()), seed]).standard_normal(out[name].shape)
        drawn = base * np.exp(spread * noise) if base else spread * noise
        out[name] = jnp.asarray(drawn.astype(out[name].dtype))
    for name, factor in factors.items():
        out[name] = (out[name] * factor).astype(out[name].dtype)
    return out
```

```python
from contextlib import ExitStack

import concourse.bass as bass
from concourse import mybir

F32 = mybir.dt.float32
F32R = mybir.dt.float32r
I32 = mybir.dt.int32
ALU = mybir.AluOpType
ACT = mybir.ActivationFunctionType

P = 128
LN_EPS = 1e-5


def adapter_program(nc, x, itok, w_down, b_down, w_up, b_up, ln_w, ln_b, out):
    B, S, H = x.shape
    E, _, BN = w_down.shape
    assert 2 * S == P and H % P == 0 and BN % P == 0 and B & (B - 1) == 0
    KH = H // P
    KB = BN // P
    TILES = (B + E - 1) // 2
    SLOTS = 2 * TILES
    CODE = E * B
    RANGE = 256
    assert CODE <= RANGE and RANGE * SLOTS < 2 ** 24
    assert TILES % 4 == 1 and TILES > 8
    DEEP = 4
    STORE_LAG = 5
    PAR = 2

    with ExitStack() as ctx:
        def sb(name, shape, dt=F32):
            return ctx.enter_context(nc.sbuf_tensor(name, shape, dt))

        def ps(name, shape, dt=F32):
            return ctx.enter_context(nc.psum_tensor(name, shape, dt))

        def sem(name):
            return ctx.enter_context(nc.semaphore(name))

        ident = sb("ident", [P, P])
        ones_r = sb("ones_r", [P, P], F32R)
        half_neg = sb("half_neg", [P, 1])
        before = sb("before", [B, B])
        slot_row = sb("slot_row", [B, SLOTS])
        batch_col = sb("batch_col", [B, 1])
        ones_col = sb("ones_col", [B, 1])
        is_row1 = sb("is_row1", [P, 1])
        sign_row = sb("sign_row", [P, 1])

        wd = sb("wd", [P, E, KH, BN])
        wd_hi = sb("wd_hi", [P, E * KH * BN], F32R)
        wd_lo = sb("wd_lo", [P, E * KH * BN], F32R)
        wu = sb("wu", [P, E, KB, H])
        wu_hi = sb("wu_hi", [P, E * KB * H], F32R)
        wu_lo = sb("wu_lo", [P, E * KB * H], F32R)
        bd = sb("bd", [2, E * BN])
        bd_hi = sb("bd_hi", [2, E * BN], F32R)
        bd_rest = sb("bd_rest", [2, E * BN])
        bd_parts = sb("bd_parts", [P, E * BN], F32R)
        bu_rows = sb("bu_rows", [P, E * H])
        lnw_rows = sb("lnw_rows", [P, E * H])
        lnb_rows = sb("lnb_rows", [P, E * H])

        itok_all_i = sb("itok_all_i", [B, B], I32)
        itok_own_i = sb("itok_own_i", [B, 1], I32)
        itok_all = sb("itok_all", [B, B])
        itok_own = sb("itok_own", [B, 1])
        sort_a = sb("sort_a", [B, B])
        sort_b = sb("sort_b", [B, E, B])
        rank = sb("rank", [B, 1])
        count = sb("count", [B, E])
        pairs_i = sb("pairs_i", [B, E], I32)
        even = sb("even", [B, E])
        ahead = sb("ahead", [B, E])
        pos = sb("pos", [B, 1])
        code_col = sb("code_col", [B, 1])
        key_col = sb("key_col", [B, 1])
        onehot = sb("onehot", [B, SLOTS])
        key_row = sb("key_row", [1, SLOTS])
        key_filled = sb("key_filled", [1, SLOTS], I32)
        slot_code = sb("slot_code", [1, 1 + SLOTS], I32)
        slot_batch = sb("slot_batch", [1, SLOTS], I32)
        slot_expert = sb("slot_expert", [1, SLOTS], I32)
        slot_code_f = sb("slot_code_f", [1, 1 + SLOTS])
        slot_new = sb("slot_new", [1, SLOTS], I32)

        xs = sb("xs", [P, DEEP, H])
        xb = sb("xb", [P, DEEP, H])
        xT_hi = sb("xT_hi", [P, PAR, KH * P], F32R)
        xT_lo = sb("xT_lo", [P, PAR, KH * P], F32R)
        g = sb("g", [P, PAR, BN])
        gT_hi = sb("gT_hi", [P, PAR, KB * P], F32R)
        gT_lo = sb("gT_lo", [P, PAR, KB * P], F32R)
        r = sb("r", [P, DEEP, H])
        r_sum = sb("r_sum", [P, DEEP])
        r_nmean = sb("r_nmean", [P, DEEP])
        sq_junk = sb("sq_junk", [P, H])
        sq_sum = sb("sq_sum", [P, DEEP])
        var_eps = sb("var_eps", [P, DEEP])
        rstd = sb("rstd", [P, DEEP])
        normed = sb("normed", [P, PAR, H])
        scaled = sb("scaled", [P, PAR, H])
        res = sb("res", [P, DEEP, H])

        xT_ps = [ps(f"xT_ps{i}", [P, KH * P]) for i in range(PAR)]
        h_ps = [ps(f"h_ps{i}", [P, 512]) for i in range(PAR)]
        gT_ps = [ps(f"gT_ps{i}", [P, 512]) for i in range(PAR)]
        y_ps = [ps(f"y_ps{i}", [P, H]) for i in range(PAR)]
        key_ps = gT_ps[1]

        itok_in = sem("itok_in")
        wd_in = sem("wd_in")
        wu_in = sem("wu_in")
        bd_in = sem("bd_in")
        bu_in = sem("bu_in")
        lnw_in = sem("lnw_in")
        lnb_in = sem("lnb_in")
        const_raw = sem("const_raw")
        const_ready = sem("const_ready")
        sorting = sem("sorting")
        key_ready = sem("key_ready")
        slots_ready = sem("slots_ready")
        w_hi_ready = sem("w_hi_ready")
        w_lo_ready = sem("w_lo_ready")
        bd_step = sem("bd_step")
        x_in = [sem(f"x_in{i}") for i in range(PAR)]
        xT_ready = sem("xT_ready")
        xhi_ready = sem("xhi_ready")
        xlo_ready = sem("xlo_ready")
        h_ready = sem("h_ready")
        g_ready = sem("g_ready")
        gT_ready = sem("gT_ready")
        ghi_ready = sem("ghi_ready")
        glo_ready = sem("glo_ready")
        y_ready = sem("y_ready")
        xb_ready = sem("xb_ready")
        r_ready = sem("r_ready")
        nmean_ready = sem("nmean_ready")
        sq_ready = sem("sq_ready")
        var_ready = sem("var_ready")
        rstd_ready = sem("rstd_ready")
        normed_ready = sem("normed_ready")
        scaled_ready = sem("scaled_ready")
        res_ready = sem("res_ready")
        stored = [sem(f"stored{i}") for i in range(PAR)]

        def ds(start, n):
            return bass.ds(start, n)

        def expert_of(eng, t):
            return eng.value_load(slot_expert[0:1, ds(2 * t, 1)], min_val=0, max_val=E - 1)

        def landed_count(t, c):
            return 32 * (t // PAR + 1) if isinstance(t, int) else t * (32 // PAR) + 32 - (32 // PAR) * (c % PAR)

        def tiles(eng, step, first, last, unroll):
            whole = (last + 1 - first) // unroll
            with eng.Fori(0, whole) as k:
                for c in range(unroll):
                    step(k * unroll + (first + c), (first + c) % unroll)
            for t in range(first + whole * unroll, last + 1):
                step(t, t % unroll)

        block = ctx.enter_context(nc.Block())

        @block.sync
        def _(sp):
            sp.dma_start(itok_all_i[:], itok.rearrange("(a b) -> a b", a=1).broadcast_to([B, B])).then_inc(itok_in, 16)
            sp.dma_start(itok_own_i[:], itok.rearrange("(b a) -> b a", a=1)).then_inc(itok_in, 16)
            sp.wait_ge(slots_ready, 1)

            def load(t, c):
                for half in range(2):
                    b = sp.value_load(slot_batch[0:1, ds(2 * t + half, 1)], min_val=0, max_val=B - 1)
                    sp.dma_start(xs[half * S:(half + 1) * S, c % DEEP, :],
                                 x[ds(b, 1), :, :].rearrange("a s h -> (a s) h")).then_inc(x_in[c % PAR], 16)

            def store(t, c):
                sp.wait_ge(res_ready, t + 1)
                if not isinstance(t, int) or t >= PAR:
                    sp.wait_ge(stored[c % PAR], landed_count(t - PAR, c))
                for half in range(2):
                    b = sp.value_load(slot_batch[0:1, ds(2 * t + half, 1)], min_val=0, max_val=B - 1)
                    new = sp.value_load(slot_new[0:1, ds(2 * t + half, 1)], min_val=0, max_val=1)
                    sp.dma_start(out[ds(b, 1), :, :].rearrange("a s h -> (a s) h"),
                                 res[half * S:(half + 1) * S, c % DEEP, :], cond=new > 0).then_inc(stored[c % PAR], 16)

            for t in range(DEEP):
                if t >= PAR:
                    sp.wait_ge(x_in[t % PAR], 32 * (t // PAR))
                load(t, t)

            def body(t, c):
                sp.wait_ge(xT_ready, t)
                sp.wait_ge(xb_ready, t)
                sp.wait_ge(x_in[(c + 1) % PAR], landed_count(t + 1, c + 1))
                load(t + DEEP - 1, c + DEEP - 1)
                if not isinstance(t, int) or t >= STORE_LAG:
                    store(t - STORE_LAG, c + 4 * DEEP - STORE_LAG)

            for t in range(1, STORE_LAG + 2):
                body(t, t)
            tiles(sp, body, STORE_LAG + 2, TILES - DEEP, 4)
            for t in range(TILES - DEEP + 1 - STORE_LAG, TILES):
                store(t, t)
            for i in range(PAR):
                sp.wait_ge(stored[i], 32 * len(range(i, TILES, PAR)))

        @block.gpsimd
        def _(pool):
            pool.memset(ident[:], 0.0).then_inc(const_raw, 1)
            pool.memset(before[:], 0.0).then_inc(const_raw, 1)
            pool.memset(half_neg[:], -0.5).then_inc(const_ready, 1)
            pool.memset(ones_col[:], 1.0).then_inc(const_ready, 1)
            pool.iota(slot_row[:], pattern=[[1, SLOTS]], base=0, channel_multiplier=0,
                      allow_small_or_imprecise_dtypes=True).then_inc(const_ready, 1)
            pool.iota(batch_col[:], pattern=[[0, 1]], base=0, channel_multiplier=1,
                      allow_small_or_imprecise_dtypes=True).then_inc(const_ready, 1)
            pool.iota(is_row1[0:2, :], pattern=[[0, 1]], base=0, channel_multiplier=1,
                      allow_small_or_imprecise_dtypes=True).then_inc(const_ready, 1)
            pool.iota(sign_row[0:2, :], pattern=[[0, 1]], base=1, channel_multiplier=-2,
                      allow_small_or_imprecise_dtypes=True).then_inc(const_ready, 1)
            pool.wait_ge(const_raw, 2)
            pool.affine_select(out=before[:], in_=before[:], compare_op=ALU.is_ge, fill=1.0, base=0,
                               pattern=[[1, B]], channel_multiplier=-1).then_inc(const_ready, 1)
            pool.affine_select(out=ident[:], in_=ident[:], compare_op=ALU.not_equal, fill=1.0, base=0,
                               pattern=[[-1, P]], channel_multiplier=1).then_inc(const_ready, 1)
            pool.wait_ge(slots_ready, 1)

            def add_bias(t, c):
                e = expert_of(pool, t)
                pool.wait_ge(x_in[c % PAR], landed_count(t, c))
                if not isinstance(t, int) or t >= DEEP:
                    pool.wait_ge(r_ready, t - DEEP + 1)
                pool.tensor_tensor(xb[:, c % DEEP, :], xs[:, c % DEEP, :], bu_rows[:, ds(e * H, H)],
                                   ALU.add).then_inc(xb_ready, 1)

            def power(t, c):
                pool.wait_ge(var_ready, t + 1)
                pool.tensor_tensor(rstd[:, c % DEEP:c % DEEP + 1], var_eps[:, c % DEEP:c % DEEP + 1], half_neg[:],
                                   ALU.pow).then_inc(rstd_ready, 1)

            def scale(t, c):
                e = expert_of(pool, t)
                pool.wait_ge(normed_ready, t + 1)
                if not isinstance(t, int) or t >= PAR:
                    pool.wait_ge(res_ready, t - PAR + 1)
                pool.tensor_tensor(scaled[:, c % PAR, :], normed[:, c % PAR, :], lnw_rows[:, ds(e * H, H)],
                                   ALU.mult).then_inc(scaled_ready, 1)

            pool.wait_ge(bu_in, 16)
            for t in range(4):
                add_bias(t, t)
            pool.wait_ge(lnw_in, 16)

            def body(t, c):
                power(t, c)
                scale(t, c)
                add_bias(t + 4, c)

            body(0, 0)
            tiles(pool, body, 1, TILES - 5, 4)
            for t in range(TILES - 4, TILES):
                power(t, t)
                scale(t, t)

        @block.scalar
        def _(act):
            act.dma_start(wd[:], w_down.rearrange("e (c p) n -> p e c n", p=P)).then_inc(wd_in, 16)
            act.dma_start(bd[:], b_down.rearrange("(a e) n -> a (e n)", a=1).broadcast_to([2, E * BN])).then_inc(bd_in, 16)
            act.dma_start(wu[:], w_up.rearrange("e (c p) n -> p e c n", p=P)).then_inc(wu_in, 16)
            for rows, vec, landed in ((bu_rows, b_up, bu_in), (lnw_rows, ln_w, lnw_in), (lnb_rows, ln_b, lnb_in)):
                act.dma_start(rows[:], vec.rearrange("(a e) h -> a (e h)", a=1).broadcast_to([P, E * H])).then_inc(landed, 16)

            def x_hi(t, c):
                act.wait_ge(xT_ready, t + 1)
                if not isinstance(t, int) or t >= PAR:
                    act.wait_ge(h_ready, t - PAR + 1)
                act.copy(xT_hi[:, c % PAR, :], xT_ps[c % PAR][:]).then_inc(xhi_ready, 1)

            def gelu(t, c):
                act.wait_ge(h_ready, t + 1)
                if not isinstance(t, int) or t >= PAR:
                    act.wait_ge(gT_ready, t - PAR + 1)
                act.activation(g[:, c % PAR, :], h_ps[c % PAR][:, 0:BN], ACT.Gelu).then_inc(g_ready, 1)

            def g_hi(t, c):
                act.wait_ge(gT_ready, t + 1)
                if not isinstance(t, int) or t >= PAR:
                    act.wait_ge(y_ready, t - PAR + 1)
                act.copy(gT_hi[:, c % PAR, :], gT_ps[c % PAR][:, 0:BN]).then_inc(ghi_ready, 1)

            def square(t, c):
                act.wait_ge(nmean_ready, t + 1)
                if not isinstance(t, int) or t >= 1:
                    act.wait_ge(sq_ready, t)
                act.activation(sq_junk[:], r[:, c % DEEP, :], ACT.Square, bias=r_nmean[:, c % DEEP:c % DEEP + 1],
                               accum_out=sq_sum[:, c % DEEP:c % DEEP + 1]).then_inc(sq_ready, 1)

            act.wait_ge(wd_in, 16)
            for e in range(E):
                act.copy(wd_hi[:, e * KH * BN:(e + 1) * KH * BN],
                         wd[:, e, :, :].rearrange("p c n -> p (c n)")).then_inc(w_hi_ready, 1)
            x_hi(0, 0)
            x_hi(1, 1)
            act.wait_ge(wu_in, 16)
            for e in range(E):
                act.copy(wu_hi[:, e * KB * H:(e + 1) * KB * H],
                         wu[:, e, :, :].rearrange("p c n -> p (c n)")).then_inc(w_hi_ready, 1)
            gelu(0, 0)
            x_hi(2, 2)

            def body(t, c):
                g_hi(t - 1, c + 3)
                gelu(t, c)
                x_hi(t + 2, c + 2)
                if not (isinstance(t, int) and t < 2):
                    square(t - 2, c + 2)

            body(1, 1)
            body(2, 2)
            body(3, 3)
            body(4, 0)
            tiles(act, body, 5, TILES - 3, 4)
            for t in (TILES - 2, TILES - 1):
                g_hi(t - 1, t - 1)
                gelu(t, t)
                square(t - 2, t - 2)
            g_hi(TILES - 1, TILES - 1)
            square(TILES - 2, TILES - 2)
            square(TILES - 1, TILES - 1)

        @block.vector
        def _(dve):
            steps = [0]

            def link(ins):
                steps[0] += 1
                ins.then_inc(sorting, 1)
                dve.wait_ge(sorting, steps[0])

            dve.memset(slot_code[0:1, 0:1], CODE)
            dve.memset(bd_parts[:].bitcast(F32), 0.0).then_inc(bd_step, 1)
            dve.memset(ones_r[:].bitcast(F32), 1.0).then_inc(bd_step, 1)
            dve.wait_ge(const_ready, 8)
            dve.wait_ge(itok_in, 32)
            dve.tensor_scalar(itok_all[:], itok_all_i[:], 0.0, float(E - 1), ALU.max, ALU.min)
            link(dve.tensor_scalar(itok_own[:], itok_own_i[:], 0.0, float(E - 1), ALU.max, ALU.min))
            dve.scalar_tensor_tensor(out=sort_a[:], in0=itok_all[:], scalar=itok_own[:], in1=before[:],
                                     op0=ALU.is_equal, op1=ALU.mult, accum_out=rank[:])
            for e in range(E - 1):
                last = dve.tensor_scalar(sort_b[:, e, :], itok_all[:], float(e), None, ALU.is_equal, ALU.add,
                                         accum_out=count[:, e:e + 1])
            link(last)
            link(dve.tensor_scalar(pairs_i[:, 0:E - 1], count[:, 0:E - 1], 0.5, 0.25, ALU.mult, ALU.add))
            link(dve.tensor_scalar(even[:, 0:E - 1], pairs_i[:, 0:E - 1], 2.0, None, ALU.mult))
            for e in range(E - 1):
                last = dve.tensor_scalar(ahead[:, e:e + 1], itok_own[:], float(e + 1), even[:, e:e + 1],
                                         ALU.is_ge, ALU.mult)
            dve.tensor_scalar(code_col[:], itok_own[:], float(B), batch_col[:], ALU.mult, ALU.add)
            link(last)
            link(dve.tensor_scalar(pos[:], rank[:], ahead[:, 0:1], ahead[:, 1:2], ALU.add, ALU.add))
            dve.tensor_scalar(key_col[:], pos[:], float(RANGE), code_col[:], ALU.mult, ALU.add)
            dve.tensor_scalar(onehot[:], slot_row[:], pos[:], None, ALU.is_equal).then_inc(key_ready, 1)
            dve.wait_ge(key_ready, 2)
            link(dve.tensor_copy(key_row[:], key_ps[0:1, 0:SLOTS]))
            link(dve.tensor_tensor_scan(key_filled[:], key_row[:], key_row[:], 0.0, ALU.max, ALU.max))
            link(dve.tensor_scalar(slot_code[:, 1:1 + SLOTS], key_filled[:], RANGE - 1, None, ALU.bitwise_and))
            dve.tensor_copy(slot_code_f[:], slot_code[:])
            dve.tensor_scalar(slot_batch[:], slot_code[:, 1:1 + SLOTS], B - 1, None, ALU.bitwise_and)
            link(dve.tensor_scalar(slot_expert[:], slot_code[:, 1:1 + SLOTS], B.bit_length() - 1, None,
                                   ALU.logical_shift_right))
            link(dve.tensor_tensor(slot_new[:], slot_code_f[:, 1:1 + SLOTS], slot_code_f[:, 0:SLOTS],
                                   ALU.not_equal))
            dve.memset(sort_a[0:1, 0:1], 0.0).then_inc(slots_ready, 1)

            dve.wait_ge(bd_in, 16)
            dve.tensor_copy(bd_hi[:], bd[:]).then_inc(bd_step, 1)
            dve.tensor_scalar(bd_rest[:], bd[:], is_row1[0:2, :], None, ALU.mult).then_inc(bd_step, 1)
            dve.wait_ge(bd_step, 4)
            dve.scalar_tensor_tensor(out=bd_parts[0:2, :], in0=bd_hi[:].bitcast(F32), scalar=sign_row[0:2, :],
                                     in1=bd_rest[:], op0=ALU.mult, op1=ALU.add).then_inc(bd_step, 1)

            for e in range(E):
                n = KH * BN
                dve.wait_ge(w_hi_ready, e + 1)
                dve.tensor_tensor(wd_lo[:, e * n:(e + 1) * n], wd[:, e, :, :].rearrange("p c n -> p (c n)"),
                                  wd_hi[:, e * n:(e + 1) * n].bitcast(F32), ALU.subtract).then_inc(w_lo_ready, 1)

            def x_lo(t, c):
                dve.wait_ge(xhi_ready, t + 1)
                if not isinstance(t, int) or t >= PAR:
                    dve.wait_ge(h_ready, t - PAR + 1)
                dve.tensor_tensor(xT_lo[:, c % PAR, :], xT_ps[c % PAR][:], xT_hi[:, c % PAR, :].bitcast(F32),
                                  ALU.subtract).then_inc(xlo_ready, 1)

            def g_lo(t, c):
                dve.wait_ge(ghi_ready, t + 1)
                if not isinstance(t, int) or t >= PAR:
                    dve.wait_ge(y_ready, t - PAR + 1)
                dve.tensor_tensor(gT_lo[:, c % PAR, :], gT_ps[c % PAR][:, 0:BN], gT_hi[:, c % PAR, :].bitcast(F32),
                                  ALU.subtract).then_inc(glo_ready, 1)

            def residual(t, c):
                dve.wait_ge(y_ready, t + 1)
                dve.wait_ge(xb_ready, t + 1)
                if not isinstance(t, int) or t >= DEEP:
                    dve.wait_ge(normed_ready, t - DEEP + 1)
                dve.scalar_tensor_tensor(out=r[:, c % DEEP, :], in0=y_ps[c % PAR][:], scalar=1.0, in1=xb[:, c % DEEP, :],
                                         op0=ALU.mult, op1=ALU.add,
                                         accum_out=r_sum[:, c % DEEP:c % DEEP + 1]).then_inc(r_ready, 1)
                dve.wait_ge(r_ready, t + 1)
                dve.tensor_scalar(r_nmean[:, c % DEEP:c % DEEP + 1], r_sum[:, c % DEEP:c % DEEP + 1], -1.0 / H, None,
                                  ALU.mult).then_inc(nmean_ready, 1)

            def variance(t, c):
                dve.wait_ge(sq_ready, t + 1)
                dve.tensor_scalar(var_eps[:, c % DEEP:c % DEEP + 1], sq_sum[:, c % DEEP:c % DEEP + 1], 1.0 / H, LN_EPS,
                                  ALU.mult, ALU.add).then_inc(var_ready, 1)

            def normalise(t, c):
                dve.wait_ge(rstd_ready, t + 1)
                if not isinstance(t, int) or t >= PAR:
                    dve.wait_ge(scaled_ready, t - PAR + 1)
                dve.tensor_scalar(normed[:, c % PAR, :], r[:, c % DEEP, :], r_nmean[:, c % DEEP:c % DEEP + 1],
                                  rstd[:, c % DEEP:c % DEEP + 1], ALU.add, ALU.mult).then_inc(normed_ready, 1)

            def shift(t, c):
                e = expert_of(dve, t)
                dve.wait_ge(scaled_ready, t + 1)
                if not isinstance(t, int) or t >= DEEP:
                    dve.wait_ge(stored[c % PAR], landed_count(t - DEEP, c))
                dve.tensor_tensor(res[:, c % DEEP, :], scaled[:, c % PAR, :], lnb_rows[:, ds(e * H, H)],
                                  ALU.add).then_inc(res_ready, 1)

            x_lo(0, 0)
            x_lo(1, 1)
            for e in range(E):
                n = KB * H
                dve.wait_ge(w_hi_ready, E + e + 1)
                dve.tensor_tensor(wu_lo[:, e * n:(e + 1) * n], wu[:, e, :, :].rearrange("p c n -> p (c n)"),
                                  wu_hi[:, e * n:(e + 1) * n].bitcast(F32), ALU.subtract).then_inc(w_lo_ready, 1)
            x_lo(2, 2)
            dve.wait_ge(lnb_in, 16)

            def body(t, c):
                first = t if isinstance(t, int) else 100
                g_lo(t - 1, c + 3)
                if first >= 3:
                    variance(t - 3, c + 1)
                if first >= 2:
                    residual(t - 2, c + 2)
                if first >= 3:
                    normalise(t - 3, c + 1)
                x_lo(t + 2, c + 2)
                if first >= 4:
                    shift(t - 4, c)

            for t in range(1, 9):
                body(t, t % 4)
            tiles(dve, body, 9, TILES - 3, 4)
            for t in range(TILES - 2, TILES + 4):
                if t <= TILES:
                    g_lo(t - 1, t - 1)
                if t - 3 < TILES:
                    variance(t - 3, t - 3)
                if t - 2 < TILES:
                    residual(t - 2, t - 2)
                if t - 3 < TILES:
                    normalise(t - 3, t - 3)
                if t - 4 < TILES:
                    shift(t - 4, t - 4)

        @block.tensor
        def _(pe):
            pe.wait_ge(key_ready, 1)
            pe.matmul(key_ps[0:1, 0:SLOTS], key_col[:], onehot[:], start=True, stop=True).then_inc(key_ready, 1)

            def transpose_x(t, c):
                pe.wait_ge(x_in[c % PAR], landed_count(t, c))
                if not isinstance(t, int) or t >= PAR:
                    pe.wait_ge(xlo_ready, t - PAR + 1)
                for k in range(KH):
                    mm = pe.transpose(xT_ps[c % PAR][:, k * P:(k + 1) * P], xs[:, c % DEEP, k * P:(k + 1) * P], ident[:])
                mm.then_inc(xT_ready, 1)

            def down(t, c):
                e = expert_of(pe, t)
                w0 = e * (KH * BN)
                if not isinstance(t, int) or t >= PAR:
                    pe.wait_ge(g_ready, t - PAR + 1)
                pe.wait_ge(xhi_ready, t + 1)
                h = h_ps[c % PAR][:, 0:BN]
                pe.matmul(h, ones_r[:], bd_parts[:, ds(e * BN, BN)], start=True, stop=False)
                for x_half, w_half in ((xT_hi, wd_hi), (xT_hi, wd_lo), (xT_lo, wd_hi)):
                    if x_half is xT_lo:
                        pe.wait_ge(xlo_ready, t + 1)
                    for k in range(KH):
                        mm = pe.matmul(h, x_half[:, c % PAR, k * P:(k + 1) * P], w_half[:, ds(w0 + k * BN, BN)],
                                       start=False, stop=(x_half is xT_lo and k == KH - 1))
                mm.then_inc(h_ready, 1)

            def transpose_g(t, c):
                pe.wait_ge(g_ready, t + 1)
                if not isinstance(t, int) or t >= PAR:
                    pe.wait_ge(glo_ready, t - PAR + 1)
                for k in range(KB):
                    mm = pe.transpose(gT_ps[c % PAR][:, k * P:(k + 1) * P], g[:, c % PAR, k * P:(k + 1) * P], ident[:])
                mm.then_inc(gT_ready, 1)

            def up(t, c):
                e = expert_of(pe, t)
                w0 = e * (KB * H)
                if not isinstance(t, int) or t >= PAR:
                    pe.wait_ge(r_ready, t - PAR + 1)
                pe.wait_ge(ghi_ready, t + 1)
                for n, (g_half, w_half) in enumerate(((gT_hi, wu_hi), (gT_hi, wu_lo), (gT_lo, wu_hi))):
                    if g_half is gT_lo:
                        pe.wait_ge(glo_ready, t + 1)
                    for k in range(KB):
                        mm = pe.matmul(y_ps[c % PAR][:], g_half[:, c % PAR, k * P:(k + 1) * P],
                                       w_half[:, ds(w0 + k * H, H)], start=(n == 0 and k == 0),
                                       stop=(n == 2 and k == KB - 1))
                mm.then_inc(y_ready, 1)

            pe.wait_ge(slots_ready, 1)
            transpose_x(0, 0)
            transpose_x(1, 1)
            pe.wait_ge(bd_step, 5)
            pe.wait_ge(w_lo_ready, E)
            down(0, 0)
            transpose_x(2, 2)
            transpose_g(0, 0)
            pe.wait_ge(w_lo_ready, 2 * E)

            def body(t, c):
                down(t, c)
                transpose_x(t + 2, c + 2)
                up(t - 1, c + 3)
                transpose_g(t, c)


            body(1, 1)
            body(2, 2)
            tiles(pe, body, 3, TILES - 3, 4)
            for t in range(TILES - 2, TILES):
                down(t, t)
                if t + 2 < TILES:
                    transpose_x(t + 2, t + 2)
                up(t - 1, t - 1)
                transpose_g(t, t)
            up(TILES - 1, TILES - 1)


_INS = ['x', 'itok_B_1_2', 'L0_cond_W_down', 'L0_cond_b_down', 'L0_cond_W_up', 'L0_cond_b_up', 'L0_cond_ln_w',
        'L0_cond_ln_b']


def kernel(**inputs):
    import numpy as _np
    import concourse.bacc as _bacc
    from concourse import mybir as _mybir
    from concourse.bass_utils import run_bass_kernel_spmd as _run

    nc = _bacc.Bacc("TRN2", target_bir_lowering=False, num_devices=1)
    arrays, args = {}, []
    for name in _INS:
        a = _np.ascontiguousarray(inputs[name])
        arrays[f"in_{name}_dram"] = a
        args.append(nc.dram_tensor(f"in_{name}_dram", a.shape, _mybir.dt.from_np(a.dtype), kind="ExternalInput").ap())
    shape = inputs['x'].shape
    args.append(nc.dram_tensor("out_dram", shape, _mybir.dt.float32, kind="ExternalOutput").ap())
    adapter_program(nc, *args)
    r = _run(nc, [arrays], core_ids=[0])
    return r.results[0]["out_dram"]
```

```python
from contextlib import ExitStack

import concourse.bass as bass
from concourse import mybir

F32 = mybir.dt.float32
F32R = mybir.dt.float32r
I32 = mybir.dt.int32
ALU = mybir.AluOpType
ACT = mybir.ActivationFunctionType

P = 128
LN_EPS = 1e-5


def adapter_program(nc, x, itok, w_down, b_down, w_up, b_up, ln_w, ln_b, out):
    B, S, H = x.shape
    E, _, BN = w_down.shape
    assert 2 * S == P and H % P == 0 and BN % P == 0 and B & (B - 1) == 0
    KH = H // P
    KB = BN // P
    TILES = (B + E - 1) // 2
    SLOTS = 2 * TILES
    CODE = E * B
    RANGE = 256
    assert CODE <= RANGE and RANGE * SLOTS < 2 ** 24
    assert TILES % 4 == 1 and TILES > 8
    DEEP = 4
    STORE_A_LAG = 9
    STORE_LAG = 5
    PAR = 2

    with ExitStack() as ctx:
        def sb(name, shape, dt=F32):
            return ctx.enter_context(nc.sbuf_tensor(name, shape, dt))

        def ps(name, shape, dt=F32):
            return ctx.enter_context(nc.psum_tensor(name, shape, dt))

        def sem(name):
            return ctx.enter_context(nc.semaphore(name))

        ident = sb("ident", [P, P])
        ones_r = sb("ones_r", [P, P], F32R)
        half_neg = sb("half_neg", [P, 1])
        before = sb("before", [B, B])
        slot_row = sb("slot_row", [B, SLOTS])
        batch_col = sb("batch_col", [B, 1])
        ones_col = sb("ones_col", [B, 1])
        is_row1 = sb("is_row1", [P, 1])
        sign_row = sb("sign_row", [P, 1])

        wd = sb("wd", [P, E, KH, BN])
        wd_hi = sb("wd_hi", [P, E * KH * BN], F32R)
        wd_lo = sb("wd_lo", [P, E * KH * BN], F32R)
        wu = sb("wu", [P, E, KB, H])
        wu_hi = sb("wu_hi", [P, E * KB * H], F32R)
        wu_lo = sb("wu_lo", [P, E * KB * H], F32R)
        bd = sb("bd", [2, E * BN])
        bd_hi = sb("bd_hi", [2, E * BN], F32R)
        bd_rest = sb("bd_rest", [2, E * BN])
        bd_parts = sb("bd_parts", [P, E * BN], F32R)
        bu_rows = sb("bu_rows", [P, E * H])
        lnw_rows = sb("lnw_rows", [P, E * H])
        lnb_rows = sb("lnb_rows", [P, E * H])

        itok_all_i = sb("itok_all_i", [B, B], I32)
        itok_own_i = sb("itok_own_i", [B, 1], I32)
        itok_all = sb("itok_all", [B, B])
        itok_own = sb("itok_own", [B, 1])
        sort_a = sb("sort_a", [B, B])
        sort_b = sb("sort_b", [B, E, B])
        rank = sb("rank", [B, 1])
        count = sb("count", [B, E])
        pairs_i = sb("pairs_i", [B, E], I32)
        even = sb("even", [B, E])
        ahead = sb("ahead", [B, E])
        pos = sb("pos", [B, 1])
        code_col = sb("code_col", [B, 1])
        key_col = sb("key_col", [B, 1])
        onehot = sb("onehot", [B, SLOTS])
        key_row = sb("key_row", [1, SLOTS])
        key_filled = sb("key_filled", [1, SLOTS], I32)
        slot_code = sb("slot_code", [1, 1 + SLOTS], I32)
        slot_batch = sb("slot_batch", [1, SLOTS], I32)
        io_table = sb("io_table", [1, 3 * (TILES + STORE_A_LAG)], I32)
        tile_expert = sb("tile_expert", [1, TILES], I32)
        slot_code_f = sb("slot_code_f", [1, 1 + SLOTS])
        slot_same = sb("slot_same", [1, SLOTS])
        slot_batch_f = sb("slot_batch_f", [1, SLOTS])
        slot_store = sb("slot_store", [1, SLOTS], I32)

        xs = sb("xs", [P, DEEP, H])
        xb = sb("xb", [P, DEEP, H])
        xT_hi = sb("xT_hi", [P, PAR, KH * P], F32R)
        xT_lo = sb("xT_lo", [P, PAR, KH * P], F32R)
        g = sb("g", [P, PAR, BN])
        gT_hi = sb("gT_hi", [P, PAR, KB * P], F32R)
        gT_lo = sb("gT_lo", [P, PAR, KB * P], F32R)
        r = sb("r", [P, DEEP, H])
        r_sum = sb("r_sum", [P, DEEP])
        r_nmean = sb("r_nmean", [P, DEEP])
        sq_junk = sb("sq_junk", [P, H])
        sq_sum = sb("sq_sum", [P, DEEP])
        var_eps = sb("var_eps", [P, DEEP])
        rstd = sb("rstd", [P, DEEP])
        normed = sb("normed", [P, PAR, H])
        scaled = sb("scaled", [P, PAR, H])
        res = sb("res", [P, DEEP, H])

        xT_ps = [ps(f"xT_ps{i}", [P, KH * P]) for i in range(PAR)]
        h_ps = [ps(f"h_ps{i}", [P, 512]) for i in range(PAR)]
        gT_ps = [ps(f"gT_ps{i}", [P, 512]) for i in range(PAR)]
        y_ps = [ps(f"y_ps{i}", [P, H]) for i in range(PAR)]
        key_ps = gT_ps[1]

        itok_in = sem("itok_in")
        wd_in = sem("wd_in")
        wu_in = sem("wu_in")
        bd_in = sem("bd_in")
        bu_in = sem("bu_in")
        lnw_in = sem("lnw_in")
        lnb_in = sem("lnb_in")
        const_raw = sem("const_raw")
        const_ready = sem("const_ready")
        sorting = sem("sorting")
        key_ready = sem("key_ready")
        slots_ready = sem("slots_ready")
        w_hi_ready = sem("w_hi_ready")
        w_lo_ready = sem("w_lo_ready")
        bd_step = sem("bd_step")
        x_in = [sem(f"x_in{i}") for i in range(DEEP)]
        xT_ready = sem("xT_ready")
        xhi_ready = sem("xhi_ready")
        xlo_ready = sem("xlo_ready")
        h_ready = sem("h_ready")
        g_ready = sem("g_ready")
        gT_ready = sem("gT_ready")
        ghi_ready = sem("ghi_ready")
        glo_ready = sem("glo_ready")
        y_ready = sem("y_ready")
        xb_ready = sem("xb_ready")
        r_ready = sem("r_ready")
        nmean_ready = sem("nmean_ready")
        sq_ready = sem("sq_ready")
        var_ready = sem("var_ready")
        rstd_ready = sem("rstd_ready")
        normed_ready = sem("normed_ready")
        scaled_ready = sem("scaled_ready")
        res_ready = sem("res_ready")
        stored = [sem(f"stored{i}") for i in range(DEEP)]

        def ds(start, n):
            return bass.ds(start, n)

        def loaded(eng, table, at, most):
            return nc.values_load(table[0:1, ds(at, 1)], engines=[eng.engine], min_val=0, max_val=most,
                                  skip_runtime_bounds_check_because="the sort clamps the experts, and so all codes")

        def expert_of(eng, t):
            return loaded(eng, tile_expert, t, E - 1)

        def landed_count(t, c):
            return 32 * (t // DEEP + 1) if isinstance(t, int) else t * (32 // DEEP) + 32 - (32 // DEEP) * (c % DEEP)

        def tiles(eng, step, first, last, unroll):
            whole = (last + 1 - first) // unroll
            with eng.Fori(0, whole) as k:
                for c in range(unroll):
                    step(k * unroll + (first + c), (first + c) % unroll)
            for t in range(first + whole * unroll, last + 1):
                step(t, t % unroll)

        block = ctx.enter_context(nc.Block())

        @block.sync
        def _(sp):
            sp.dma_start(itok_all_i[:], itok.rearrange("(a b) -> a b", a=1).broadcast_to([B, B])).then_inc(itok_in, 16)
            sp.dma_start(itok_own_i[:], itok.rearrange("(b a) -> b a", a=1)).then_inc(itok_in, 16)
            sp.wait_ge(slots_ready, 2)

            io_regs = [sp.alloc_register(f"io{i}") for i in range(3)]

            def entries(t, first, n):
                sp.reg_load(io_regs[:n], io_table[0:1, ds(3 * t + first, n)])
                return [sp.snap(reg, min_val=0, max_val=B - 1) for reg in io_regs[:n]]

            def load(t, c, batches):
                if not isinstance(t, int) or t >= DEEP:
                    sp.wait_ge(xT_ready, t - DEEP + 1)
                    sp.wait_ge(xb_ready, t - DEEP + 1)
                for half in range(2):
                    sp.dma_start(xs[half * S:(half + 1) * S, c % DEEP, :],
                                 x[ds(batches[half], 1), :, :].rearrange("a s h -> (a s) h")).then_inc(x_in[c % DEEP], 16)

            def store(t, c, batch):
                sp.wait_ge(res_ready, t + 1)
                sp.dma_start(out[ds(batch, 1), :, :].rearrange("a s h -> (a s) h"), res[0:S, c % DEEP, :],
                             bounds_check="skip_entire_dma").then_inc(stored[c % DEEP], 16)

            for t in range(STORE_A_LAG):
                load(t, t, entries(t, 0, 2))

            sp.wait_ge(slots_ready, 3)

            def body(t, c):
                batch_a, batch_b, out_a = entries(t, 0, 3)
                load(t, c, (batch_a, batch_b))
                store(t - STORE_A_LAG, c + 4 * DEEP - STORE_A_LAG, out_a)

            tiles(sp, body, STORE_A_LAG, TILES - 1, 4)
            for t in range(TILES - STORE_A_LAG, TILES):
                store(t, t, *entries(t + STORE_A_LAG, 2, 1))
            for i in range(DEEP):
                sp.wait_ge(stored[i], 32 * len(range(i, TILES, DEEP)))

        @block.gpsimd
        def _(pool):
            pool.memset(ident[:], 0.0).then_inc(const_raw, 1)
            pool.memset(before[:], 0.0).then_inc(const_raw, 1)
            pool.memset(half_neg[:], -0.5).then_inc(const_ready, 1)
            pool.memset(ones_col[:], 1.0).then_inc(const_ready, 1)
            pool.iota(slot_row[:], pattern=[[1, SLOTS]], base=0, channel_multiplier=0,
                      allow_small_or_imprecise_dtypes=True).then_inc(const_ready, 1)
            pool.iota(batch_col[:], pattern=[[0, 1]], base=0, channel_multiplier=1,
                      allow_small_or_imprecise_dtypes=True).then_inc(const_ready, 1)
            pool.iota(is_row1[0:2, :], pattern=[[0, 1]], base=0, channel_multiplier=1,
                      allow_small_or_imprecise_dtypes=True).then_inc(const_ready, 1)
            pool.iota(sign_row[0:2, :], pattern=[[0, 1]], base=1, channel_multiplier=-2,
                      allow_small_or_imprecise_dtypes=True).then_inc(const_ready, 1)
            pool.wait_ge(const_raw, 2)
            pool.affine_select(out=before[:], in_=before[:], compare_op=ALU.is_ge, fill=1.0, base=0,
                               pattern=[[1, B]], channel_multiplier=-1).then_inc(const_ready, 1)
            pool.affine_select(out=ident[:], in_=ident[:], compare_op=ALU.not_equal, fill=1.0, base=0,
                               pattern=[[-1, P]], channel_multiplier=1).then_inc(const_ready, 1)
            pool.wait_ge(slots_ready, 2)

            def add_bias(t, c):
                e = expert_of(pool, t)
                pool.wait_ge(x_in[c % DEEP], landed_count(t, c))
                if not isinstance(t, int) or t >= DEEP:
                    pool.wait_ge(r_ready, t - DEEP + 1)
                pool.tensor_tensor(xb[:, c % DEEP, :], xs[:, c % DEEP, :], bu_rows[:, ds(e * H, H)],
                                   ALU.add).then_inc(xb_ready, 1)

            def power(t, c):
                pool.wait_ge(var_ready, t + 1)
                pool.tensor_tensor(rstd[:, c % DEEP:c % DEEP + 1], var_eps[:, c % DEEP:c % DEEP + 1], half_neg[:],
                                   ALU.pow).then_inc(rstd_ready, 1)

            def scale(t, c):
                e = expert_of(pool, t)
                pool.wait_ge(normed_ready, t + 1)
                if not isinstance(t, int) or t >= PAR:
                    pool.wait_ge(res_ready, t - PAR + 1)
                pool.tensor_tensor(scaled[:, c % PAR, :], normed[:, c % PAR, :], lnw_rows[:, ds(e * H, H)],
                                   ALU.mult).then_inc(scaled_ready, 1)

            pool.wait_ge(bu_in, 16)
            for t in range(4):
                add_bias(t, t)
            pool.wait_ge(lnw_in, 16)

            def body(t, c):
                power(t, c)
                scale(t, c)
                add_bias(t + 4, c)

            body(0, 0)
            tiles(pool, body, 1, TILES - 5, 4)
            for t in range(TILES - 4, TILES):
                power(t, t)
                scale(t, t)

        @block.scalar
        def _(act):
            act.dma_start(wd[:], w_down.rearrange("e (c p) n -> p e c n", p=P)).then_inc(wd_in, 16)
            act.dma_start(bd[:], b_down.rearrange("(a e) n -> a (e n)", a=1).broadcast_to([2, E * BN])).then_inc(bd_in, 16)
            act.dma_start(wu[:], w_up.rearrange("e (c p) n -> p e c n", p=P)).then_inc(wu_in, 16)
            for rows, vec, landed in ((bu_rows, b_up, bu_in), (lnw_rows, ln_w, lnw_in), (lnb_rows, ln_b, lnb_in)):
                act.dma_start(rows[:], vec.rearrange("(a e) h -> a (e h)", a=1).broadcast_to([P, E * H])).then_inc(landed, 16)

            def store(t, c):
                batch = nc.values_load(slot_store[0:1, ds(2 * t + 1, 1)], engines=[act.engine], min_val=0, max_val=B - 1,
                                       skip_runtime_bounds_check_because="the DMA checks it: beyond B - 1 it skips")
                act.wait_ge(res_ready, t + 1)
                act.dma_start(out[ds(batch, 1), :, :].rearrange("a s h -> (a s) h"), res[S:P, c % DEEP, :],
                              bounds_check="skip_entire_dma").then_inc(stored[c % DEEP], 16)

            def x_hi(t, c):
                act.wait_ge(xT_ready, t + 1)
                act.copy(xT_hi[:, c % PAR, :], xT_ps[c % PAR][:]).then_inc(xhi_ready, 1)

            def gelu(t, c):
                act.wait_ge(h_ready, t + 1)
                act.activation(g[:, c % PAR, :], h_ps[c % PAR][:, 0:BN], ACT.Gelu).then_inc(g_ready, 1)

            def g_hi(t, c):
                act.wait_ge(gT_ready, t + 1)
                act.copy(gT_hi[:, c % PAR, :], gT_ps[c % PAR][:, 0:BN]).then_inc(ghi_ready, 1)

            def square(t, c):
                act.wait_ge(nmean_ready, t + 1)
                if not isinstance(t, int) or t >= 1:
                    act.wait_ge(sq_ready, t)
                act.activation(sq_junk[:], r[:, c % DEEP, :], ACT.Square, bias=r_nmean[:, c % DEEP:c % DEEP + 1],
                               accum_out=sq_sum[:, c % DEEP:c % DEEP + 1]).then_inc(sq_ready, 1)

            act.wait_ge(wd_in, 16)
            for e in range(E):
                act.copy(wd_hi[:, e * KH * BN:(e + 1) * KH * BN],
                         wd[:, e, :, :].rearrange("p c n -> p (c n)")).then_inc(w_hi_ready, 1)
            x_hi(0, 0)
            x_hi(1, 1)
            act.wait_ge(wu_in, 16)
            for e in range(E):
                act.copy(wu_hi[:, e * KB * H:(e + 1) * KB * H],
                         wu[:, e, :, :].rearrange("p c n -> p (c n)")).then_inc(w_hi_ready, 1)
            gelu(0, 0)
            x_hi(2, 2)

            def body(t, c):
                g_hi(t - 1, c + 3)
                if not isinstance(t, int) or t >= STORE_LAG:
                    store(t - STORE_LAG, c + 4 * DEEP - STORE_LAG)
                gelu(t, c)
                x_hi(t + 2, c + 2)
                if not isinstance(t, int) or t >= 2:
                    square(t - 2, c + 2)

            act.wait_ge(slots_ready, 3)
            for t in range(1, STORE_LAG + 2):
                body(t, t)
            tiles(act, body, STORE_LAG + 2, TILES - 3, 4)
            for t in range(TILES - 2, TILES + STORE_LAG):
                if t - 1 < TILES:
                    g_hi(t - 1, t - 1)
                if t < TILES:
                    gelu(t, t)
                if t - 2 < TILES:
                    square(t - 2, t - 2)
                store(t - STORE_LAG, t - STORE_LAG)

        @block.vector
        def _(dve):
            steps = [0]

            def link(ins):
                steps[0] += 1
                ins.then_inc(sorting, 1)
                dve.wait_ge(sorting, steps[0])

            dve.memset(slot_code[0:1, 0:1], CODE)
            dve.memset(bd_parts[:].bitcast(F32), 0.0).then_inc(bd_step, 1)
            dve.memset(ones_r[:].bitcast(F32), 1.0).then_inc(bd_step, 1)
            dve.wait_ge(const_ready, 8)
            dve.wait_ge(itok_in, 32)
            dve.tensor_scalar(itok_all[:], itok_all_i[:], 0.0, float(E - 1), ALU.max, ALU.min)
            link(dve.tensor_scalar(itok_own[:], itok_own_i[:], 0.0, float(E - 1), ALU.max, ALU.min))
            dve.scalar_tensor_tensor(out=sort_a[:], in0=itok_all[:], scalar=itok_own[:], in1=before[:],
                                     op0=ALU.is_equal, op1=ALU.mult, accum_out=rank[:])
            for e in range(E - 1):
                last = dve.tensor_scalar(sort_b[:, e, :], itok_all[:], float(e), None, ALU.is_equal, ALU.add,
                                         accum_out=count[:, e:e + 1])
            link(last)
            link(dve.tensor_scalar(pairs_i[:, 0:E - 1], count[:, 0:E - 1], 0.5, 0.25, ALU.mult, ALU.add))
            link(dve.tensor_scalar(even[:, 0:E - 1], pairs_i[:, 0:E - 1], 2.0, None, ALU.mult))
            for e in range(E - 1):
                last = dve.tensor_scalar(ahead[:, e:e + 1], itok_own[:], float(e + 1), even[:, e:e + 1],
                                         ALU.is_ge, ALU.mult)
            dve.tensor_scalar(code_col[:], itok_own[:], float(B), batch_col[:], ALU.mult, ALU.add)
            link(last)
            link(dve.tensor_scalar(pos[:], rank[:], ahead[:, 0:1], ahead[:, 1:2], ALU.add, ALU.add))
            dve.tensor_scalar(key_col[:], pos[:], float(RANGE), code_col[:], ALU.mult, ALU.add)
            dve.tensor_scalar(onehot[:], slot_row[:], pos[:], None, ALU.is_equal).then_inc(key_ready, 1)
            dve.wait_ge(key_ready, 2)
            link(dve.tensor_copy(key_row[:], key_ps[0:1, 0:SLOTS]))
            link(dve.tensor_tensor_scan(key_filled[:], key_row[:], key_row[:], 0.0, ALU.max, ALU.max))
            link(dve.tensor_scalar(slot_code[:, 1:1 + SLOTS], key_filled[:], RANGE - 1, None, ALU.bitwise_and))
            dve.tensor_copy(slot_code_f[:], slot_code[:])
            dve.tensor_scalar(tile_expert[:], slot_code[:, 1:1 + SLOTS:2], B.bit_length() - 1, None,
                              ALU.logical_shift_right).then_inc(slots_ready, 1)
            link(dve.tensor_scalar(slot_batch[:], slot_code[:, 1:1 + SLOTS], B - 1, None, ALU.bitwise_and))
            dve.tensor_copy(slot_batch_f[:], slot_batch[:])
            io_view = io_table[:].rearrange("p (t n) -> p t n", n=3)
            dve.tensor_copy(io_view[:, 0:TILES, 0:2],
                            slot_batch[:].rearrange("p (t n) -> p t n", n=2)).then_inc(slots_ready, 1)
            link(dve.tensor_tensor(slot_same[:], slot_code_f[:, 1:1 + SLOTS], slot_code_f[:, 0:SLOTS], ALU.is_equal))
            link(dve.scalar_tensor_tensor(out=slot_store[:], in0=slot_same[:], scalar=float(B), in1=slot_batch_f[:],
                                     op0=ALU.mult, op1=ALU.add))
            dve.tensor_copy(io_view[:, STORE_A_LAG:, 2], slot_store[:, 0:SLOTS:2]).then_inc(slots_ready, 1)

            dve.wait_ge(bd_in, 16)
            dve.tensor_copy(bd_hi[:], bd[:]).then_inc(bd_step, 1)
            dve.tensor_scalar(bd_rest[:], bd[:], is_row1[0:2, :], None, ALU.mult).then_inc(bd_step, 1)
            dve.wait_ge(bd_step, 4)
            dve.scalar_tensor_tensor(out=bd_parts[0:2, :], in0=bd_hi[:].bitcast(F32), scalar=sign_row[0:2, :],
                                     in1=bd_rest[:], op0=ALU.mult, op1=ALU.add).then_inc(bd_step, 1)

            for e in range(E):
                n = KH * BN
                dve.wait_ge(w_hi_ready, e + 1)
                dve.tensor_tensor(wd_lo[:, e * n:(e + 1) * n], wd[:, e, :, :].rearrange("p c n -> p (c n)"),
                                  wd_hi[:, e * n:(e + 1) * n].bitcast(F32), ALU.subtract).then_inc(w_lo_ready, 1)

            def x_lo(t, c):
                dve.wait_ge(xhi_ready, t + 1)
                dve.tensor_tensor(xT_lo[:, c % PAR, :], xT_ps[c % PAR][:], xT_hi[:, c % PAR, :].bitcast(F32),
                                  ALU.subtract).then_inc(xlo_ready, 1)

            def g_lo(t, c):
                dve.wait_ge(ghi_ready, t + 1)
                dve.tensor_tensor(gT_lo[:, c % PAR, :], gT_ps[c % PAR][:, 0:BN], gT_hi[:, c % PAR, :].bitcast(F32),
                                  ALU.subtract).then_inc(glo_ready, 1)

            def residual(t, c):
                dve.wait_ge(y_ready, t + 1)
                dve.wait_ge(xb_ready, t + 1)
                dve.scalar_tensor_tensor(out=r[:, c % DEEP, :], in0=y_ps[c % PAR][:], scalar=1.0, in1=xb[:, c % DEEP, :],
                                         op0=ALU.mult, op1=ALU.add,
                                         accum_out=r_sum[:, c % DEEP:c % DEEP + 1]).then_inc(r_ready, 1)
                dve.wait_ge(r_ready, t + 1)
                dve.tensor_scalar(r_nmean[:, c % DEEP:c % DEEP + 1], r_sum[:, c % DEEP:c % DEEP + 1], -1.0 / H, None,
                                  ALU.mult).then_inc(nmean_ready, 1)

            def variance(t, c):
                dve.wait_ge(sq_ready, t + 1)
                dve.tensor_scalar(var_eps[:, c % DEEP:c % DEEP + 1], sq_sum[:, c % DEEP:c % DEEP + 1], 1.0 / H, LN_EPS,
                                  ALU.mult, ALU.add).then_inc(var_ready, 1)

            def normalise(t, c):
                dve.wait_ge(rstd_ready, t + 1)
                if not isinstance(t, int) or t >= PAR:
                    dve.wait_ge(scaled_ready, t - PAR + 1)
                dve.tensor_scalar(normed[:, c % PAR, :], r[:, c % DEEP, :], r_nmean[:, c % DEEP:c % DEEP + 1],
                                  rstd[:, c % DEEP:c % DEEP + 1], ALU.add, ALU.mult).then_inc(normed_ready, 1)

            def shift(t, c):
                e = expert_of(dve, t)
                dve.wait_ge(scaled_ready, t + 1)
                if not isinstance(t, int) or t >= DEEP:
                    dve.wait_ge(stored[c % DEEP], landed_count(t - DEEP, c))
                dve.tensor_tensor(res[:, c % DEEP, :], scaled[:, c % PAR, :], lnb_rows[:, ds(e * H, H)],
                                  ALU.add).then_inc(res_ready, 1)

            x_lo(0, 0)
            x_lo(1, 1)
            for e in range(E):
                n = KB * H
                dve.wait_ge(w_hi_ready, E + e + 1)
                dve.tensor_tensor(wu_lo[:, e * n:(e + 1) * n], wu[:, e, :, :].rearrange("p c n -> p (c n)"),
                                  wu_hi[:, e * n:(e + 1) * n].bitcast(F32), ALU.subtract).then_inc(w_lo_ready, 1)
            x_lo(2, 2)
            dve.wait_ge(lnb_in, 16)

            def body(t, c):
                first = t if isinstance(t, int) else 100
                g_lo(t - 1, c + 3)
                if first >= 3:
                    variance(t - 3, c + 1)
                if first >= 2:
                    residual(t - 2, c + 2)
                if first >= 3:
                    normalise(t - 3, c + 1)
                x_lo(t + 2, c + 2)
                if first >= 4:
                    shift(t - 4, c)

            for t in range(1, 9):
                body(t, t % 4)
            tiles(dve, body, 9, TILES - 3, 4)
            for t in range(TILES - 2, TILES + 4):
                if t <= TILES:
                    g_lo(t - 1, t - 1)
                if t - 3 < TILES:
                    variance(t - 3, t - 3)
                if t - 2 < TILES:
                    residual(t - 2, t - 2)
                if t - 3 < TILES:
                    normalise(t - 3, t - 3)
                if t - 4 < TILES:
                    shift(t - 4, t - 4)

        @block.tensor
        def _(pe):
            pe.wait_ge(key_ready, 1)
            pe.matmul(key_ps[0:1, 0:SLOTS], key_col[:], onehot[:], start=True, stop=True).then_inc(key_ready, 1)

            expert_regs = [pe.alloc_register(f"expert{i}") for i in range(2)]

            def experts_from(t):
                pe.reg_load(expert_regs, tile_expert[0:1, ds(t, 2)])
                return [pe.snap(reg, min_val=0, max_val=E - 1) for reg in expert_regs]

            def transpose_x(t, c):
                pe.wait_ge(x_in[c % DEEP], landed_count(t, c))
                for k in range(KH):
                    mm = pe.transpose(xT_ps[c % PAR][:, k * P:(k + 1) * P], xs[:, c % DEEP, k * P:(k + 1) * P], ident[:])
                mm.then_inc(xT_ready, 1)

            def down(t, c, e):
                w0 = e * (KH * BN)
                pe.wait_ge(xlo_ready, t + 1)
                h = h_ps[c % PAR][:, 0:BN]
                pe.matmul(h, ones_r[:], bd_parts[:, ds(e * BN, BN)], start=True, stop=False)
                for x_half, w_half in ((xT_hi, wd_hi), (xT_hi, wd_lo), (xT_lo, wd_hi)):
                    for k in range(KH):
                        mm = pe.matmul(h, x_half[:, c % PAR, k * P:(k + 1) * P], w_half[:, ds(w0 + k * BN, BN)],
                                       start=False, stop=(x_half is xT_lo and k == KH - 1))
                mm.then_inc(h_ready, 1)

            def transpose_g(t, c):
                pe.wait_ge(g_ready, t + 1)
                for k in range(KB):
                    mm = pe.transpose(gT_ps[c % PAR][:, k * P:(k + 1) * P], g[:, c % PAR, k * P:(k + 1) * P], ident[:])
                mm.then_inc(gT_ready, 1)

            def up(t, c, e):
                w0 = e * (KB * H)
                if not isinstance(t, int) or t >= PAR:
                    pe.wait_ge(r_ready, t - PAR + 1)
                pe.wait_ge(glo_ready, t + 1)
                for n, (g_half, w_half) in enumerate(((gT_hi, wu_hi), (gT_hi, wu_lo), (gT_lo, wu_hi))):
                    for k in range(KB):
                        mm = pe.matmul(y_ps[c % PAR][:], g_half[:, c % PAR, k * P:(k + 1) * P],
                                       w_half[:, ds(w0 + k * H, H)], start=(n == 0 and k == 0),
                                       stop=(n == 2 and k == KB - 1))
                mm.then_inc(y_ready, 1)

            pe.wait_ge(slots_ready, 2)
            transpose_x(0, 0)
            transpose_x(1, 1)
            pe.wait_ge(bd_step, 5)
            pe.wait_ge(w_lo_ready, E)
            down(0, 0, expert_of(pe, 0))
            transpose_x(2, 2)
            e0, e1 = experts_from(0)
            transpose_g(0, 0)
            down(1, 1, e1)
            transpose_x(3, 3)
            pe.wait_ge(w_lo_ready, 2 * E)
            up(0, 0, e0)

            def body(t, c):
                e_up, e_down = experts_from(t)
                transpose_g(t, c)
                down(t + 1, c + 1, e_down)
                if not isinstance(t, int) or t + 3 < TILES:
                    transpose_x(t + 3, c + 3)
                up(t, c, e_up)

            body(1, 1)
            tiles(pe, body, 2, TILES - 4, 4)
            body(TILES - 3, TILES - 3)
            body(TILES - 2, TILES - 2)
            e_up = expert_of(pe, TILES - 1)
            transpose_g(TILES - 1, TILES - 1)
            up(TILES - 1, TILES - 1, e_up)


_INS = ['x', 'itok_B_1_2', 'L0_cond_W_down', 'L0_cond_b_down', 'L0_cond_W_up', 'L0_cond_b_up', 'L0_cond_ln_w',
        'L0_cond_ln_b']


def kernel(**inputs):
    import numpy as _np
    import concourse.bacc as _bacc
    from concourse import mybir as _mybir
    from concourse.bass_utils import run_bass_kernel_spmd as _run

    nc = _bacc.Bacc("TRN2", target_bir_lowering=False, num_devices=1)
    arrays, args = {}, []
    for name in _INS:
        a = _np.ascontiguousarray(inputs[name])
        arrays[f"in_{name}_dram"] = a
        args.append(nc.dram_tensor(f"in_{name}_dram", a.shape, _mybir.dt.from_np(a.dtype), kind="ExternalInput").ap())
    shape = inputs['x'].shape
    args.append(nc.dram_tensor("out_dram", shape, _mybir.dt.float32, kind="ExternalOutput").ap())
    adapter_program(nc, *args)
    r = _run(nc, [arrays], core_ids=[0])
    return r.results[0]["out_dram"]
```

```python
from contextlib import ExitStack

import concourse.bass as bass
from concourse import mybir

F32 = mybir.dt.float32
F32R = mybir.dt.float32r
I32 = mybir.dt.int32
ALU = mybir.AluOpType
ACT = mybir.ActivationFunctionType

P = 128
LN_EPS = 1e-5


def adapter_program(nc, x, itok, w_down, b_down, w_up, b_up, ln_w, ln_b, out):
    B, S, H = x.shape
    E, _, BN = w_down.shape
    assert 2 * S == P and H % P == 0 and BN % P == 0 and B & (B - 1) == 0
    assert E == 3
    KH = H // P
    KB = BN // P
    TILES = (B + E - 1) // 2
    SLOTS = 2 * TILES
    RANGE = 1 << (E * B - 1).bit_length()
    assert RANGE * SLOTS < 2 ** 24
    TO_EVEN = 1.5 * 2 ** 24
    FAR = 8
    DEEP = 4
    PAR = 2
    UNROLL = FAR
    STORE_A_LAG = FAR + 6
    STORE_B_LAG = 5
    EARLY = 3
    WARM_UPS_BEFORE, WARM_UPS_AFTER = 11, 3

    with ExitStack() as ctx:
        def sb(name, shape, dt=F32):
            return ctx.enter_context(nc.sbuf_tensor(name, shape, dt))

        def ps(name, shape, dt=F32):
            return ctx.enter_context(nc.psum_tensor(name, shape, dt))

        def sem(name):
            return ctx.enter_context(nc.semaphore(name))

        ident = sb("ident", [P, P])
        half_neg = sb("half_neg", [P, 1])
        gelu_junk = sb("gelu_junk", [P, 1])
        before = sb("before", [B, B])
        slot_row = sb("slot_row", [B, SLOTS])
        batch_col = sb("batch_col", [B, 1])

        wd = sb("wd", [P, E, KH, BN])
        wd_hi = sb("wd_hi", [P, E * KH * BN], F32R)
        wd_lo = sb("wd_lo", [P, E * KH * BN], F32R)
        wu = sb("wu", [P, E, KB, H])
        wu_hi = sb("wu_hi", [P, E * KB * H], F32R)
        wu_lo = sb("wu_lo", [P, E * KB * H], F32R)
        bd_rows = sb("bd_rows", [P, E * BN])
        bu_rows = sb("bu_rows", [P, E * H])
        lnw_rows = sb("lnw_rows", [P, E * H])
        lnb_rows = sb("lnb_rows", [P, E * H])

        itok_all_i = sb("itok_all_i", [B, B], I32)
        itok_all = sb("itok_all", [B, B])
        itok_own = sb("itok_own", [B, 1])
        own_only = sb("own_only", [B, B])
        same_before = sb("same_before", [B, B])
        rank = sb("rank", [B, 1])
        of_expert = sb("of_expert", [B, E - 1, B])
        count = sb("count", [B, E - 1])
        even_count = sb("even_count", [B, E - 1])
        behind = sb("behind", [B, E - 1])
        slots_before = sb("slots_before", [B, E - 1])
        ahead = sb("ahead", [B, 1])
        pos = sb("pos", [B, 1])
        code = sb("code", [B, 1])
        key_col = sb("key_col", [B, 1])
        onehot = sb("onehot", [B, SLOTS])
        zero_row = sb("zero_row", [1, SLOTS])
        key_filled = sb("key_filled", [1, 1 + SLOTS], I32)
        key_f = sb("key_f", [1, 1 + SLOTS])
        slot_batch = sb("slot_batch", [1, SLOTS], I32)
        slot_batch_f = sb("slot_batch_f", [1, SLOTS])
        slot_same = sb("slot_same", [1, SLOTS])
        slot_store = sb("slot_store", [1, SLOTS], I32)
        io_table = sb("io_table", [1, 3 * (TILES + STORE_A_LAG)], I32)
        tile_expert = sb("tile_expert", [1, TILES], I32)

        x_sb = sb("x_sb", [P, FAR, H])
        xb = sb("xb", [P, DEEP, H])
        xT_hi = sb("xT_hi", [P, PAR, KH * P], F32R)
        xT_lo = sb("xT_lo", [P, PAR, KH * P], F32R)
        hb = sb("hb", [P, PAR, BN])
        g = sb("g", [P, PAR, BN])
        gT_hi = sb("gT_hi", [P, PAR, KB * P], F32R)
        gT_lo = sb("gT_lo", [P, PAR, KB * P], F32R)
        r = sb("r", [P, DEEP, H])
        r_sum = sb("r_sum", [P, DEEP])
        r_nmean = sb("r_nmean", [P, DEEP])
        sq_junk = sb("sq_junk", [P, H])
        sq_sum = sb("sq_sum", [P, DEEP])
        var_eps = sb("var_eps", [P, DEEP])
        rstd = sb("rstd", [P, DEEP])
        centred = sb("centred", [P, PAR, H])
        scaled = sb("scaled", [P, DEEP, H])
        res = sb("res", [P, FAR, H])

        xT_ps = [ps(f"xT_ps{i}", [P, KH * P]) for i in range(PAR)]
        h_ps = [ps(f"h_ps{i}", [P, 512]) for i in range(PAR)]
        gT_ps = [ps(f"gT_ps{i}", [P, 512]) for i in range(PAR)]
        y_ps = [ps(f"y_ps{i}", [P, H]) for i in range(PAR)]
        key_ps = gT_ps[1]

        itok_in = sem("itok_in")
        wd_in = [sem(f"wd_in{e}") for e in range(E)]
        wu_in = [sem(f"wu_in{e}") for e in range(E)]
        bd_in = sem("bd_in")
        bu_in = sem("bu_in")
        lnw_in = sem("lnw_in")
        lnb_in = sem("lnb_in")
        const_raw = sem("const_raw")
        const_ready = sem("const_ready")
        sorting = sem("sorting")
        key_ready = sem("key_ready")
        slots_ready = sem("slots_ready")
        w_hi_ready = sem("w_hi_ready")
        wd_lo_ready = sem("wd_lo_ready")
        wu_lo_ready = sem("wu_lo_ready")
        x_in = [sem(f"x_in{i}") for i in range(FAR)]
        xT_ready = sem("xT_ready")
        xhi_ready = sem("xhi_ready")
        xlo_ready = sem("xlo_ready")
        h_ready = sem("h_ready")
        hb_ready = sem("hb_ready")
        g_ready = sem("g_ready")
        gT_ready = sem("gT_ready")
        ghi_ready = sem("ghi_ready")
        glo_ready = sem("glo_ready")
        y_ready = sem("y_ready")
        xb_ready = sem("xb_ready")
        r_ready = sem("r_ready")
        nmean_ready = sem("nmean_ready")
        sq_ready = sem("sq_ready")
        var_ready = sem("var_ready")
        rstd_ready = sem("rstd_ready")
        centred_ready = sem("centred_ready")
        scaled_ready = sem("scaled_ready")
        last_scaled = sem("last_scaled")
        res_ready = sem("res_ready")
        stored = [sem(f"stored{i}") for i in range(FAR)]

        def ds(start, n):
            return bass.ds(start, n)

        def expert_of(eng, t):
            return nc.values_load(tile_expert[0:1, ds(t, 1)], engines=[eng.engine], min_val=0, max_val=E - 1,
                                  skip_runtime_bounds_check_because="the sort clamps the experts")

        def landed_count(t, c):
            return 32 * (t // FAR + 1) if isinstance(t, int) else t * (32 // FAR) + 32 - (32 // FAR) * (c % FAR)

        def tiles(eng, step, first, last):
            whole = (last + 1 - first) // UNROLL
            with eng.Fori(0, whole) as k:
                for c in range(UNROLL):
                    step(k * UNROLL + (first + c), (first + c) % UNROLL)
            for t in range(first + whole * UNROLL, last + 1):
                step(t, t % UNROLL)

        def from_tile(t, n):
            return not isinstance(t, int) or t >= n

        def exists(t):
            return not isinstance(t, int) or 0 <= t < TILES

        def rows_of(vector, rows):
            flat = vector if len(vector.shape) == 1 else vector.rearrange("e n -> (e n)")
            return flat.rearrange("(a n) -> a n", a=1).broadcast_to([rows, flat.shape[0]])

        def load_w_down(eng, e):
            eng.dma_start(wd[:, e, :, :], w_down[e].rearrange("(c p) n -> p c n", p=P)).then_inc(wd_in[e], 16)

        def load_w_up(eng, e):
            eng.dma_start(wu[:, e, :, :], w_up[e].rearrange("(c p) n -> p c n", p=P)).then_inc(wu_in[e], 16)

        def w_down_low(eng, e):
            part = slice(e * KH * BN, (e + 1) * KH * BN)
            return eng.tensor_tensor(wd_lo[:, part], wd[:, e, :, :].rearrange("p c n -> p (c n)"),
                                     wd_hi[:, part].bitcast(F32), ALU.subtract)

        def w_up_low(eng, e):
            part = slice(e * KB * H, (e + 1) * KB * H)
            return eng.tensor_tensor(wu_lo[:, part], wu[:, e, :, :].rearrange("p c n -> p (c n)"),
                                     wu_hi[:, part].bitcast(F32), ALU.subtract)

        block = ctx.enter_context(nc.Block())

        @block.sync
        def _(sp):
            sp.dma_start(itok_all_i[:], rows_of(itok, B)).then_inc(itok_in, 16)
            load_w_down(sp, 1)
            load_w_up(sp, 0)
            sp.wait_ge(slots_ready, 2)

            last_regs = [sp.alloc_register(f"last{i}") for i in range(2 * EARLY - 1)]
            io_regs = [sp.alloc_register(f"io{i}") for i in range(3)]

            def entries(t, first, n):
                sp.reg_load(io_regs[:n], io_table[0:1, ds(3 * t + first, n)])
                return [sp.snap(reg, min_val=0, max_val=B - 1) for reg in io_regs[:n]]

            def load(t, c, batches):
                if from_tile(t, FAR):
                    sp.wait_ge(xT_ready, t - FAR + 1)
                    sp.wait_ge(xb_ready, t - FAR + 1)
                for half in range(2):
                    batch = x[ds(batches[half], 1), :, :].rearrange("a s h -> (a s) h")
                    sp.dma_start(x_sb[half * S:(half + 1) * S, c % FAR, :], batch).then_inc(x_in[c % FAR], 16)

            def store(t, c, batch):
                sp.wait_ge(res_ready, t + 1)
                sp.dma_start(out[ds(batch, 1), :, :].rearrange("a s h -> (a s) h"), res[0:S, c % FAR, :],
                             bounds_check="skip_entire_dma").then_inc(stored[c % FAR], 16)

            load(0, 0, entries(0, 0, 2))
            load_w_up(sp, 1)
            load(1, 1, entries(1, 0, 2))
            sp.dma_start(bd_rows[:], rows_of(b_down, P)).then_inc(bd_in, 16)
            load_w_up(sp, 2)
            load(2, 2, entries(2, 0, 2))
            sp.dma_start(bu_rows[:], rows_of(b_up, P)).then_inc(bu_in, 16)
            load(3, 3, entries(3, 0, 2))
            load(4, 4, entries(4, 0, 2))
            sp.dma_start(lnw_rows[:], rows_of(ln_w, P)).then_inc(lnw_in, 16)
            load(5, 5, entries(5, 0, 2))
            load(6, 6, entries(6, 0, 2))
            sp.dma_start(lnb_rows[:], rows_of(ln_b, P)).then_inc(lnb_in, 16)
            for t in range(7, STORE_A_LAG):
                load(t, t, entries(t, 0, 2))

            sp.wait_ge(slots_ready, 3)

            def body(t, c):
                batch_a, batch_b, out_a = entries(t, 0, 3)
                load(t, c, (batch_a, batch_b))
                store(t - STORE_A_LAG, c - STORE_A_LAG, out_a)

            tiles(sp, body, STORE_A_LAG, TILES - 1)
            sp.reg_load(last_regs, slot_store[0:1, SLOTS - 2 * EARLY:SLOTS - 1])
            for t in range(TILES - STORE_A_LAG, TILES - EARLY):
                store(t, t, *entries(t + STORE_A_LAG, 2, 1))
            for i in range(EARLY):
                t = TILES - EARLY + i
                store(t, t, sp.snap(last_regs[2 * i], min_val=0, max_val=B - 1))
            for i in range(FAR):
                sp.wait_ge(stored[i], 32 * len(range(i, TILES, FAR)))

        @block.gpsimd
        def _(pool):
            pool.memset(ident[:], 0.0).then_inc(const_raw, 1)
            pool.memset(before[:], 0.0).then_inc(const_raw, 1)
            pool.memset(half_neg[:], -0.5).then_inc(const_ready, 1)
            pool.iota(slot_row[:], pattern=[[1, SLOTS]], base=0, channel_multiplier=0,
                      allow_small_or_imprecise_dtypes=True).then_inc(const_ready, 1)
            pool.iota(batch_col[:], pattern=[[0, 1]], base=0, channel_multiplier=1,
                      allow_small_or_imprecise_dtypes=True).then_inc(const_ready, 1)
            pool.wait_ge(const_raw, 2)
            pool.affine_select(out=before[:], in_=before[:], compare_op=ALU.is_ge, fill=1.0, base=0,
                               pattern=[[1, B]], channel_multiplier=-1).then_inc(const_ready, 1)
            pool.affine_select(out=ident[:], in_=ident[:], compare_op=ALU.not_equal, fill=1.0, base=0,
                               pattern=[[-1, P]], channel_multiplier=1).then_inc(const_ready, 1)
            for e in range(E - 1):
                pool.wait_ge(w_hi_ready, e + 1)
                w_down_low(pool, e).then_inc(wd_lo_ready, 1)
            pool.wait_ge(w_hi_ready, E + 2)
            w_up_low(pool, 1).then_inc(wu_lo_ready, 1)
            pool.wait_ge(slots_ready, 2)

            def add_bias(t, c):
                e = expert_of(pool, t)
                pool.wait_ge(x_in[c % FAR], landed_count(t, c))
                if from_tile(t, DEEP):
                    pool.wait_ge(r_ready, t - DEEP + 1)
                pool.tensor_tensor(xb[:, c % DEEP, :], x_sb[:, c % FAR, :], bu_rows[:, ds(e * H, H)],
                                   ALU.add).then_inc(xb_ready, 1)

            def power(t, c):
                pool.wait_ge(var_ready, t + 1)
                pool.tensor_tensor(rstd[:, c % DEEP:c % DEEP + 1], var_eps[:, c % DEEP:c % DEEP + 1], half_neg[:],
                                   ALU.pow).then_inc(rstd_ready, 1)

            def scale(t, c):
                e = expert_of(pool, t)
                pool.wait_ge(centred_ready, t + 1)
                if from_tile(t, DEEP):
                    pool.wait_ge(res_ready, t - DEEP + 1)
                pool.tensor_tensor(scaled[:, c % DEEP, :], centred[:, c % PAR, :], lnw_rows[:, ds(e * H, H)],
                                   ALU.mult).then_inc(scaled_ready, 1)

            pool.wait_ge(bu_in, 16)
            for t in range(DEEP):
                add_bias(t, t)
            pool.wait_ge(lnw_in, 16)

            def body(t, c):
                scale(t, c)
                power(t, c)
                add_bias(t + DEEP, c + DEEP)

            for t in range(DEEP + 1):
                body(t, t)
            tiles(pool, body, DEEP + 1, TILES - 1 - DEEP)
            for t in range(TILES - DEEP, TILES):
                if t < TILES - 2:
                    scale(t, t)
                power(t, t)

        @block.scalar
        def _(act):
            load_w_down(act, 0)
            load_w_down(act, 2)
            act.wait_ge(const_ready, 1)
            act.activation(gelu_junk[:], half_neg[:], ACT.Gelu)

            def place(t):
                return nc.values_load(slot_store[0:1, ds(2 * t + 1, 1)], engines=[act.engine], min_val=0,
                                      max_val=B - 1,
                                      skip_runtime_bounds_check_because="the DMA skips what is beyond B - 1")

            def store(t, c, batch=None):
                if batch is None:
                    batch = place(t)
                act.wait_ge(res_ready, t + 1)
                act.dma_start(out[ds(batch, 1), :, :].rearrange("a s h -> (a s) h"), res[S:P, c % FAR, :],
                              bounds_check="skip_entire_dma").then_inc(stored[c % FAR], 16)

            def x_hi(t, c):
                act.wait_ge(xT_ready, t + 1)
                act.copy(xT_hi[:, c % PAR, :], xT_ps[c % PAR][:]).then_inc(xhi_ready, 1)

            def gelu(t, c):
                act.wait_ge(hb_ready, t + 1)
                act.activation(g[:, c % PAR, :], hb[:, c % PAR, :], ACT.Gelu).then_inc(g_ready, 1)

            def g_hi(t, c):
                act.wait_ge(gT_ready, t + 1)
                act.copy(gT_hi[:, c % PAR, :], gT_ps[c % PAR][:, 0:BN]).then_inc(ghi_ready, 1)

            def square(t, c):
                act.wait_ge(nmean_ready, t + 1)
                if from_tile(t, 1):
                    act.wait_ge(sq_ready, t)
                act.activation(sq_junk[:], r[:, c % DEEP, :], ACT.Square, bias=r_nmean[:, c % DEEP:c % DEEP + 1],
                               accum_out=sq_sum[:, c % DEEP:c % DEEP + 1]).then_inc(sq_ready, 1)

            def centre(t, c):
                act.wait_ge(nmean_ready, t + 1)
                if from_tile(t, PAR):
                    act.wait_ge(scaled_ready, t - PAR + 1)
                act.activation(centred[:, c % PAR, :], r[:, c % DEEP, :], ACT.Identity,
                               bias=r_nmean[:, c % DEEP:c % DEEP + 1]).then_inc(centred_ready, 1)

            for e in range(E):
                act.wait_ge(wd_in[e], 16)
                act.copy(wd_hi[:, e * KH * BN:(e + 1) * KH * BN],
                         wd[:, e, :, :].rearrange("p c n -> p (c n)")).then_inc(w_hi_ready, 1)

            def wu_high(e):
                act.wait_ge(wu_in[e], 16)
                act.copy(wu_hi[:, e * KB * H:(e + 1) * KB * H],
                         wu[:, e, :, :].rearrange("p c n -> p (c n)")).then_inc(w_hi_ready, 1)

            wu_high(0)
            x_hi(0, 0)
            wu_high(1)
            x_hi(1, 1)
            gelu(0, 0)
            wu_high(2)
            g_hi(0, 0)
            x_hi(2, 2)

            def body(t, c):
                if from_tile(t, 2):
                    g_hi(t - 1, c - 1)
                if from_tile(t, STORE_B_LAG):
                    store(t - STORE_B_LAG, c - STORE_B_LAG)
                if from_tile(t, 2):
                    square(t - 2, c - 2)
                gelu(t, c)
                x_hi(t + 2, c + 2)
                if from_tile(t, 2):
                    centre(t - 2, c - 2)

            act.wait_ge(slots_ready, 3)
            last_places = [place(t) for t in range(TILES - EARLY, TILES)]
            for t in range(1, STORE_B_LAG + 2):
                body(t, t)
            tiles(act, body, STORE_B_LAG + 2, TILES - 3)
            last = TILES - 1
            g_hi(last - 2, last - 2)
            square(last - 3, last - 3)
            gelu(last - 1, last - 1)
            centre(last - 3, last - 3)
            g_hi(last - 1, last - 1)
            store(last - 6, last - 6)
            centre(last - 2, last - 2)
            square(last - 2, last - 2)
            gelu(last, last)
            store(last - 5, last - 5)
            g_hi(last, last)
            store(last - 4, last - 4)
            square(last - 1, last - 1)
            store(last - 3, last - 3)
            square(last, last)
            for t, batch in zip(range(TILES - EARLY, TILES), last_places):
                store(t, t, batch)

        @block.vector
        def _(dve):
            steps = [0]

            def link(ins):
                steps[0] += 1
                ins.then_inc(sorting, 1)
                dve.wait_ge(sorting, steps[0])

            dve.memset(key_filled[0:1, 0:1], -1)
            dve.memset(zero_row[:], 0.0)
            dve.wait_ge(const_ready, 5)
            dve.wait_ge(itok_in, 16)
            link(dve.tensor_scalar(itok_all[:], itok_all_i[:], 0.0, float(E - 1), ALU.max, ALU.min))
            link(dve.scalar_tensor_tensor(out=own_only[:], in0=itok_all[:], scalar=1.0, in1=ident[0:B, 0:B],
                                          op0=ALU.mult, op1=ALU.mult, accum_out=itok_own[:]))
            dve.scalar_tensor_tensor(out=same_before[:], in0=itok_all[:], scalar=itok_own[:], in1=before[:],
                                     op0=ALU.is_equal, op1=ALU.mult, accum_out=rank[:])
            for e in range(E - 1):
                dve.tensor_scalar(behind[:, e:e + 1], itok_own[:], float(e + 1), None, ALU.is_ge)
            for e in range(E - 1):
                last = dve.tensor_scalar(of_expert[:, e, :], itok_all[:], float(e), None, ALU.is_equal, ALU.add,
                                         accum_out=count[:, e:e + 1])
            link(last)
            link(dve.tensor_scalar(even_count[:], count[:], 0.5, TO_EVEN, ALU.add, ALU.add))
            dve.tensor_scalar(code[:], itok_own[:], float(B), batch_col[:], ALU.mult, ALU.add)
            link(dve.scalar_tensor_tensor(out=slots_before[:], in0=even_count[:], scalar=-TO_EVEN, in1=behind[:],
                                          op0=ALU.add, op1=ALU.mult, accum_out=ahead[:]))
            link(dve.tensor_tensor(pos[:], rank[:], ahead[:], ALU.add))
            dve.tensor_scalar(key_col[:], pos[:], float(RANGE), code[:], ALU.mult, ALU.add)
            dve.tensor_scalar(onehot[:], slot_row[:], pos[:], None, ALU.is_equal).then_inc(key_ready, 1)
            dve.wait_ge(key_ready, 2)
            link(dve.tensor_tensor_scan(key_filled[:, 1:1 + SLOTS], key_ps[0:1, 0:SLOTS], zero_row[:], 0.0,
                                        ALU.max, ALU.max))
            io_view = io_table[:].rearrange("p (t n) -> p t n", n=3)
            dve.tensor_scalar(io_view[:, 0:TILES, 0:2], key_filled[:, 1:1 + SLOTS].rearrange("p (t n) -> p t n", n=2),
                              B - 1, None, ALU.bitwise_and).then_inc(slots_ready, 1)
            dve.tensor_scalar(tile_expert[:], key_filled[:, 1:1 + SLOTS:2], B.bit_length() - 1, RANGE // B - 1,
                              ALU.logical_shift_right, ALU.bitwise_and).then_inc(slots_ready, 1)
            dve.tensor_copy(key_f[:], key_filled[:])
            link(dve.tensor_scalar(slot_batch[:], key_filled[:, 1:1 + SLOTS], B - 1, None, ALU.bitwise_and))
            link(dve.tensor_copy(slot_batch_f[:], slot_batch[:]))
            link(dve.tensor_tensor(slot_same[:], key_f[:, 1:1 + SLOTS], key_f[:, 0:SLOTS], ALU.is_equal))
            link(dve.scalar_tensor_tensor(out=slot_store[:], in0=slot_same[:], scalar=float(B), in1=slot_batch_f[:],
                                     op0=ALU.mult, op1=ALU.add))
            dve.tensor_copy(io_view[:, STORE_A_LAG:, 2], slot_store[:, 0:SLOTS:2]).then_inc(slots_ready, 1)

            dve.wait_ge(slots_ready, 3)
            e_last = [expert_of(dve, TILES - 1 - i) for i in range(EARLY)]
            dve.wait_ge(w_hi_ready, E)
            w_down_low(dve, E - 1).then_inc(wd_lo_ready, 1)

            def x_lo(t, c):
                dve.wait_ge(xhi_ready, t + 1)
                dve.tensor_tensor(xT_lo[:, c % PAR, :], xT_ps[c % PAR][:], xT_hi[:, c % PAR, :].bitcast(F32),
                                  ALU.subtract).then_inc(xlo_ready, 1)

            def down_bias(t, c):
                e = expert_of(dve, t)
                dve.wait_ge(h_ready, t + 1)
                dve.tensor_tensor(hb[:, c % PAR, :], h_ps[c % PAR][:, 0:BN], bd_rows[:, ds(e * BN, BN)],
                                  ALU.add).then_inc(hb_ready, 1)

            def g_lo(t, c):
                dve.wait_ge(ghi_ready, t + 1)
                dve.tensor_tensor(gT_lo[:, c % PAR, :], gT_ps[c % PAR][:, 0:BN], gT_hi[:, c % PAR, :].bitcast(F32),
                                  ALU.subtract).then_inc(glo_ready, 1)

            def residual(t, c):
                dve.wait_ge(y_ready, t + 1)
                dve.wait_ge(xb_ready, t + 1)
                dve.scalar_tensor_tensor(out=r[:, c % DEEP, :], in0=y_ps[c % PAR][:], scalar=1.0,
                                         in1=xb[:, c % DEEP, :], op0=ALU.mult, op1=ALU.add,
                                         accum_out=r_sum[:, c % DEEP:c % DEEP + 1]).then_inc(r_ready, 1)

            def minus_mean(t, c):
                dve.wait_ge(r_ready, t + 1)
                dve.tensor_scalar(r_nmean[:, c % DEEP:c % DEEP + 1], r_sum[:, c % DEEP:c % DEEP + 1], -1.0 / H, None,
                                  ALU.mult).then_inc(nmean_ready, 1)

            def variance(t, c):
                dve.wait_ge(sq_ready, t + 1)
                dve.tensor_scalar(var_eps[:, c % DEEP:c % DEEP + 1], sq_sum[:, c % DEEP:c % DEEP + 1], 1.0 / H, LN_EPS,
                                  ALU.mult, ALU.add).then_inc(var_ready, 1)

            def scale_last(t, e):
                dve.wait_ge(nmean_ready, t + 1)
                dve.wait_ge(res_ready, t - DEEP + 1)
                dve.scalar_tensor_tensor(out=scaled[:, t % DEEP, :], in0=r[:, t % DEEP, :],
                                         scalar=r_nmean[:, t % DEEP:t % DEEP + 1], in1=lnw_rows[:, ds(e * H, H)],
                                         op0=ALU.add, op1=ALU.mult).then_inc(last_scaled, 1)

            def shift(t, c, e=None):
                if isinstance(t, int) and t == 0:
                    dve.wait_ge(lnb_in, 16)
                if e is None:
                    e = expert_of(dve, t)
                if isinstance(t, int) and t >= TILES - 2:
                    dve.wait_ge(last_scaled, t - (TILES - 2) + 1)
                else:
                    dve.wait_ge(scaled_ready, t + 1)
                dve.wait_ge(rstd_ready, t + 1)
                if from_tile(t, FAR):
                    dve.wait_ge(stored[c % FAR], landed_count(t - FAR, c))
                dve.scalar_tensor_tensor(out=res[:, c % FAR, :], in0=scaled[:, c % DEEP, :],
                                         scalar=rstd[:, c % DEEP:c % DEEP + 1], in1=lnb_rows[:, ds(e * H, H)],
                                         op0=ALU.mult, op1=ALU.add).then_inc(res_ready, 1)

            def wu_low(e):
                dve.wait_ge(w_hi_ready, E + e + 1)
                w_up_low(dve, e).then_inc(wu_lo_ready, 1)

            x_lo(0, 0)
            wu_low(0)
            dve.wait_ge(bd_in, 16)
            down_bias(0, 0)
            x_lo(1, 1)
            wu_low(2)
            g_lo(0, 0)
            down_bias(1, 1)
            x_lo(2, 2)

            def body(t, c):
                if exists(t - 1):
                    residual(t - 1, c - 1)
                if exists(t - 2):
                    variance(t - 2, c - 2)
                if exists(t):
                    g_lo(t, c)
                if exists(t - 1):
                    minus_mean(t - 1, c - 1)
                if exists(t + 1):
                    down_bias(t + 1, c + 1)
                if exists(t + 2):
                    x_lo(t + 2, c + 2)
                if exists(t - 3):
                    shift(t - 3, c - 3)

            for t in range(1, 11):
                body(t, t % UNROLL)
            tiles(dve, body, 11, TILES - 3)
            body(TILES - 2, TILES - 2)
            last = TILES - 1
            residual(last - 1, last - 1)
            variance(last - 2, last - 2)
            shift(last - 3, last - 3)
            minus_mean(last - 1, last - 1)
            g_lo(last, last)
            scale_last(last - 1, e_last[1])
            shift(last - 2, last - 2, e_last[2])
            variance(last - 1, last - 1)
            residual(last, last)
            minus_mean(last, last)
            shift(last - 1, last - 1, e_last[1])
            variance(last, last)
            scale_last(last, e_last[0])
            shift(last, last, e_last[0])

        @block.tensor
        def _(pe):
            pe.wait_ge(key_ready, 1)
            pe.matmul(key_ps[0:1, 0:SLOTS], key_col[:], onehot[:], start=True, stop=True).then_inc(key_ready, 1)

            def warm_up(times):
                for _ in range(times):
                    pe.matmul(h_ps[1][:, 0:P], ident[:], ident[:], start=True, stop=True)

            warm_up(WARM_UPS_BEFORE)

            expert_regs = [pe.alloc_register(f"expert{i}") for i in range(2)]

            def experts_from(t):
                pe.reg_load(expert_regs, tile_expert[0:1, ds(t, 2)])
                return [pe.snap(reg, min_val=0, max_val=E - 1) for reg in expert_regs]

            def transpose_x(t, c):
                pe.wait_ge(x_in[c % FAR], landed_count(t, c))
                for k in range(KH):
                    chunk = slice(k * P, (k + 1) * P)
                    mm = pe.transpose(xT_ps[c % PAR][:, chunk], x_sb[:, c % FAR, chunk], ident[:])
                mm.then_inc(xT_ready, 1)

            def down(t, c, e):
                w0 = e * (KH * BN)
                pe.wait_ge(xhi_ready, t + 1)
                h = h_ps[c % PAR][:, 0:BN]
                for x_half, w_half in ((xT_hi, wd_hi), (xT_hi, wd_lo), (xT_lo, wd_hi)):
                    if x_half is xT_lo:
                        pe.wait_ge(xlo_ready, t + 1)
                    for k in range(KH):
                        mm = pe.matmul(h, x_half[:, c % PAR, k * P:(k + 1) * P], w_half[:, ds(w0 + k * BN, BN)],
                                       start=(w_half is wd_hi and x_half is xT_hi and k == 0),
                                       stop=(x_half is xT_lo and k == KH - 1))
                mm.then_inc(h_ready, 1)

            def transpose_g(t, c):
                pe.wait_ge(g_ready, t + 1)
                for k in range(KB):
                    mm = pe.transpose(gT_ps[c % PAR][:, k * P:(k + 1) * P], g[:, c % PAR, k * P:(k + 1) * P], ident[:])
                mm.then_inc(gT_ready, 1)

            def up(t, c, e):
                w0 = e * (KB * H)
                if from_tile(t, PAR):
                    pe.wait_ge(r_ready, t - PAR + 1)
                pe.wait_ge(ghi_ready, t + 1)
                if isinstance(t, int) and t == 0:
                    pe.wait_ge(w_hi_ready, 2 * E)
                for n, (g_half, w_half) in enumerate(((gT_hi, wu_hi), (gT_hi, wu_lo), (gT_lo, wu_hi))):
                    if isinstance(t, int) and t == 0 and n == 1:
                        pe.wait_ge(wu_lo_ready, E)
                    if g_half is gT_lo:
                        pe.wait_ge(glo_ready, t + 1)
                    for k in range(KB):
                        mm = pe.matmul(y_ps[c % PAR][:], g_half[:, c % PAR, k * P:(k + 1) * P],
                                       w_half[:, ds(w0 + k * H, H)], start=(n == 0 and k == 0),
                                       stop=(n == 2 and k == KB - 1))
                mm.then_inc(y_ready, 1)

            pe.wait_ge(slots_ready, 2)
            transpose_x(0, 0)
            warm_up(WARM_UPS_AFTER)
            pe.wait_ge(wd_lo_ready, E)
            down(0, 0, expert_of(pe, 0))
            transpose_x(1, 1)
            e0, e1 = experts_from(0)
            transpose_g(0, 0)
            down(1, 1, e1)
            transpose_x(2, 2)
            up(0, 0, e0)
            transpose_x(3, 3)

            def body(t, c):
                e_up, e_down = experts_from(t)
                transpose_g(t, c)
                down(t + 1, c + 1, e_down)
                if exists(t + 3):
                    transpose_x(t + 3, c + 3)
                up(t, c, e_up)

            body(1, 1)
            tiles(pe, body, 2, TILES - 4)
            body(TILES - 3, TILES - 3)
            body(TILES - 2, TILES - 2)
            e_up = expert_of(pe, TILES - 1)
            transpose_g(TILES - 1, TILES - 1)
            up(TILES - 1, TILES - 1, e_up)


_INS = ['x', 'itok_B_1_2', 'L0_cond_W_down', 'L0_cond_b_down', 'L0_cond_W_up', 'L0_cond_b_up', 'L0_cond_ln_w',
        'L0_cond_ln_b']


def kernel(**inputs):
    import numpy as _np
    import concourse.bacc as _bacc
    from concourse import mybir as _mybir
    from concourse.bass_utils import run_bass_kernel_spmd as _run

    nc = _bacc.Bacc("TRN2", target_bir_lowering=False, num_devices=1)
    arrays, args = {}, []
    for name in _INS:
        a = _np.ascontiguousarray(inputs[name])
        arrays[f"in_{name}_dram"] = a
        args.append(nc.dram_tensor(f"in_{name}_dram", a.shape, _mybir.dt.from_np(a.dtype), kind="ExternalInput").ap())
    shape = inputs['x'].shape
    args.append(nc.dram_tensor("out_dram", shape, _mybir.dt.float32, kind="ExternalOutput").ap())
    adapter_program(nc, *args)
    r = _run(nc, [arrays], core_ids=[0])
    return r.results[0]["out_dram"]
```
